# Optimizing a Trainium2 kernel written in Bass

```python
import numpy as np
import jax
import jax.numpy as jnp

def _softmax(x, axis=-1):
    return jax.nn.softmax(x, axis=axis)

def _gelu(x):
    return jax.nn.gelu(x, approximate=True)

def _silu(x):
    return jax.nn.silu(x)

def _sigmoid(x):
    return jax.nn.sigmoid(x)

def _layernorm(x, axis=-1, eps=1e-05):
    m = jnp.mean(x, axis=axis, keepdims=True)
    v = jnp.var(x, axis=axis, keepdims=True)
    return (x - m) / jnp.sqrt(v + eps)

def _scatter_add(tgt, idx, src, axis=0):
    return tgt.at[idx].add(src)

def _segment_sum(src, seg, n):
    return jax.ops.segment_sum(src, seg, n)
kernel_name = 'mk_rec_standalone_d1_rec_r8_e301df'

def setup_inputs(seed: int=0):
    np.random.seed(seed)
    _w = jnp.asarray

    def _rec_inputs():
        import jax
        import jax.numpy as jnp
        _rk = jax.random.key(seed)
        r_x = -0.000392918 + 0.999932 * jax.random.normal(jax.random.fold_in(_rk, 1), (2048, 32, 64), jnp.float32)
        return r_x
    r_x = _rec_inputs()

    def _L0_rec_setup():
        import jax, jax.numpy as jnp
        import numpy as np
        B, F, E = (1024, 32, 64)
        key = jax.random.key(seed)
        k1, k2 = jax.random.split(key)
        x = jax.random.normal(k1, (B, F, E), dtype=jnp.float32)
        W = jax.random.normal(k2, (E, E), dtype=jnp.float32) * (1.0 / np.sqrt(E))
        return {'x': x, 'W': W}
    _L0_rec_all = _L0_rec_setup()
    _L0_rec_in = {k: v for k, v in _L0_rec_all.items() if k in ('W',)}
    del _L0_rec_all
    return {'r_x': r_x, 'L0_rec_W': _L0_rec_in['W']}

def reference(r_x, L0_rec_W):
    import jax
    import jax.numpy as jnp

    def _L0_rec_ref(x, W):
        import jax, jax.numpy as jnp
        import numpy as np
        B, F, E = (1024, 32, 64)
        f = x.shape[1]
        i_idx, j_idx = jnp.triu_indices(f, k=1)
        xw = jnp.einsum('bfe,ed->bfd', x, W)
        return xw[:, i_idx, :] * x[:, j_idx, :]
    y = _L0_rec_ref(r_x, L0_rec_W)
    return y

_drawn_inputs = setup_inputs


def setup_inputs(seed=0):
    import zlib

    import numpy as np

    out = dict(_drawn_inputs(seed))
    spreads = {}
    factors = {}
    for name, (base, spread) in spreads.items():
        noise = np.random.default_rng([zlib.crc32(name.encode()), seed]).standard_normal(out[name].shape)
        drawn = base * np.exp(spread * noise) if base else spread * noise
        out[name] = jnp.asarray(drawn.astype(out[name].dtype))
    for name, factor in factors.items():
        out[name] = (out[name] * factor).astype(out[name].dtype)
    return out
```

```python
from contextlib import ExitStack

import concourse.bass as bass
from concourse import mybir

ALU = mybir.AluOpType
F32 = mybir.dt.float32

LANES = 128
ROWS = 2
GROUP = 2
SLOTS = 8
CUTS = (0, 8, 16, 32)


def pair_pieces(F, chunk_pairs):
    chunks = [[] for _ in range(F * (F - 1) // 2 // chunk_pairs)]
    at = 0
    for i in range(F - 1):
        j = i + 1
        while j < F:
            place = at % chunk_pairs
            n = min(F - j, chunk_pairs - place)
            chunks[at // chunk_pairs].append((i, j, n, place))
            at += n
            j += n
    return chunks


def pairwise_interaction_kernel(nc: bass.Bass, x: bass.AP, W: bass.AP, out: bass.AP):
    B, F, E = x.shape
    PAIRS = F * (F - 1) // 2
    TILES = B // (LANES * ROWS)
    GROUPS = F // GROUP
    CHUNK = F - 1
    CHUNKS = PAIRS // CHUNK
    LAPS = CHUNKS // SLOTS
    PARTS = len(CUTS) - 1
    EARLY = CUTS[-2] - 1
    chunks = pair_pieces(F, CHUNK)
    assert B % (LANES * ROWS * 2) == 0 and PAIRS % CHUNK == 0 and CHUNKS % SLOTS == 0
    BANK = 512
    assert 2 * E == LANES and ROWS * GROUP * E <= BANK and F % GROUP == 0 and TILES >= 4
    assert CUTS[0] == 0 and CUTS[-1] == F and all(cut % GROUP == 0 for cut in CUTS)

    x_tiles = x.rearrange("(t r p) f e -> t p r f e", p=LANES, r=ROWS)
    out_tiles = out.rearrange("(t r p) q e -> t p r (q e)", p=LANES, r=ROWS)

    with ExitStack() as ctx:
        def sb(name, shape):
            return ctx.enter_context(nc.sbuf_tensor(name, shape, F32))

        def psum(name, shape):
            return ctx.enter_context(nc.psum_tensor(name, shape, F32))

        def sem(name):
            return ctx.enter_context(nc.semaphore(name))

        x_sb = [sb(f"x_sb{n}", [LANES, ROWS, F, E]) for n in range(2)]
        xw_sb = [sb(f"xw_sb{n}", [LANES, ROWS, F, E]) for n in range(2)]
        out_ring = [sb(f"out_ring{n}", [LANES, ROWS, CHUNK * E]) for n in range(SLOTS)]
        W_sb = sb("W_sb", [LANES, E])
        identity = sb("identity", [LANES, LANES])
        xT_sb = [sb(f"xT_sb{n}", [LANES, ROWS, GROUP // 2, LANES]) for n in range(2)]
        xT_ps = [psum(f"xT_ps{n}", [LANES, ROWS, GROUP // 2, LANES]) for n in range(2)]
        xw_bank = [[psum(f"xw_bank{n}_{odd}", [LANES, BANK]) for odd in range(2)] for n in range(2)]
        xw_ps = [[bank[:, 0:ROWS * GROUP // 2 * E].rearrange("p (r m e) -> p r m e", r=ROWS, e=E) for bank in banks]
                 for banks in xw_bank]

        W_landed = sem("W_landed")
        identity_zeroed = sem("identity_zeroed")
        identity_ready = sem("identity_ready")
        x_landed = [[sem(f"x_landed{n}_{part}") for part in range(PARTS)] for n in range(2)]
        transposed = sem("transposed")
        xT_copied = sem("xT_copied")
        projected = sem("projected")
        xw_copied = sem("xw_copied")
        chunk_ready = sem("chunk_ready")
        early_ready = sem("early_ready")
        early_stored = sem("early_stored")
        stored = [sem(f"stored{n}") for n in range(SLOTS)]

        block = ctx.enter_context(nc.Block())

        @block.gpsimd
        def _(pool):
            nc.gpsimd.memset(identity[:], 0.0).then_inc(identity_zeroed, 1)
            pool.wait_ge(identity_zeroed, 1)
            nc.gpsimd.affine_select(out=identity[:], in_=identity[:], compare_op=ALU.not_equal, fill=1.0,
                                    base=0, pattern=[[-1, LANES]], channel_multiplier=1).then_inc(identity_ready, 1)

        @block.sync
        def _(sp):
            def load_x(t, buf):
                for part in range(PARTS):
                    f0, f1 = CUTS[part:part + 2]
                    sp.dma_start(x_sb[buf][:, :, f0:f1, :],
                                 x_tiles[t, :, :, f0:f1, :]).then_inc(x_landed[buf][part], 16)

            def store_chunk(t, c, skip=0):
                sp.wait_ge(chunk_ready, t * CHUNKS + c + 1)
                sp.dma_start(out_tiles[t, :, :, (c * CHUNK + skip) * E:(c + 1) * CHUNK * E],
                             out_ring[c % SLOTS][:, :, skip * E:]).then_inc(stored[c % SLOTS], 16)

            def store_then_load(k, buf, first=False):
                t = 2 * k + buf
                for c in range(CHUNKS):
                    store_chunk(t, c, skip=EARLY if first and c == 0 else 0)
                load_x(t + 2, buf)

            load_x(0, 0)
            load_x(1, 1)
            sp.wait_ge(early_ready, 1)
            sp.dma_start(out_tiles[0, :, :, 0:EARLY * E],
                         out_ring[0][:, :, 0:EARLY * E]).then_inc(early_stored, 16)
            for buf in range(2):
                store_then_load(0, buf, first=buf == 0)
            with sp.Fori(1, TILES // 2 - 1) as k:
                for buf in range(2):
                    store_then_load(k, buf)
            for t in range(TILES - 2, TILES):
                for c in range(CHUNKS):
                    store_chunk(t, c)
            sp.wait_ge(early_stored, 16)
            for slot in range(SLOTS):
                sp.wait_ge(stored[slot], 16 * TILES * LAPS)

        @block.tensor
        def _(pe):
            def tile(k, buf, first):
                t = 2 * k + buf

                def transpose_group(g):
                    if g * GROUP in CUTS:
                        pe.wait_ge(x_landed[buf][CUTS.index(g * GROUP)], 16 * (k + 1))
                    for r in range(ROWS):
                        for m in range(GROUP // 2):
                            f = g * GROUP + 2 * m
                            two = x_sb[buf][:, r, f:f + 2, :].rearrange("p f e -> p (f e)")
                            last = nc.tensor.transpose(xT_ps[g % 2][:, r, m, :], two, identity[:])
                    last.then_inc(transposed, 1)

                def project_group(g):
                    pe.wait_ge(xT_copied, t * GROUPS + g + 1)
                    if not (first and g < 2):
                        pe.wait_ge(xw_copied, 2 * (t * GROUPS + max(g - 1, 0)))
                    for r in range(ROWS):
                        for m in range(GROUP // 2):
                            for odd in range(2):
                                rows = slice(odd * E, (odd + 1) * E)
                                last = nc.tensor.matmul(xw_ps[g % 2][odd][:, r, m, :],
                                                        xT_sb[g % 2][rows, r, m, :], W_sb[rows, :],
                                                        start=True, stop=True)
                    last.then_inc(projected, 1)

                transpose_group(0)
                for g in range(GROUPS):
                    if g + 1 < GROUPS:
                        transpose_group(g + 1)
                    if first and g == 0:
                        pe.wait_ge(W_landed, 32)
                    project_group(g)

            pe.wait_ge(identity_ready, 1)
            for buf in range(2):
                tile(0, buf, first=buf == 0)
            with pe.Fori(1, TILES // 2) as k:
                for buf in range(2):
                    tile(k, buf, first=False)

        @block.scalar
        def _(act):
            def tile(k, buf, first):
                t = 2 * k + buf

                def copy_xT(g):
                    act.wait_ge(transposed, t * GROUPS + g + 1)
                    nc.scalar.copy(xT_sb[g % 2][:], xT_ps[g % 2][:]).then_inc(xT_copied, 1)

                def copy_xw(g):
                    act.wait_ge(projected, t * GROUPS + g + 1)
                    for odd in range(2):
                        nc.scalar.copy(xw_sb[buf][:, :, g * GROUP + odd:(g + 1) * GROUP:2, :],
                                       xw_ps[g % 2][odd]).then_inc(xw_copied, 1)

                copy_xT(0)
                for g in range(GROUPS):
                    if g + 1 < GROUPS:
                        copy_xT(g + 1)
                    copy_xw(g)
                if not first:
                    act.wait_ge(chunk_ready, t * CHUNKS)

            for odd in range(2):
                act.dma_start(W_sb[odd * E:(odd + 1) * E, :], W).then_inc(W_landed, 16)
            for buf in range(2):
                tile(0, buf, first=buf == 0)
            with act.Fori(1, TILES // 2) as k:
                for buf in range(2):
                    tile(k, buf, first=False)

        @block.vector
        def _(dve):
            def tile(k, buf, first):
                t = 2 * k + buf

                def multiply(slot, i, j, n, place):
                    return nc.vector.tensor_tensor(
                        slot[:, :, place:place + n, :],
                        xw_sb[buf][:, :, i:i + 1, :].to_broadcast([LANES, ROWS, n, E]),
                        x_sb[buf][:, :, j:j + n, :], ALU.mult)

                for c in range(CHUNKS):
                    if not (first and c < SLOTS):
                        dve.wait_ge(stored[c % SLOTS], 16 * (t * LAPS + c // SLOTS))
                    if first and c == SLOTS:
                        dve.wait_ge(early_stored, 16)
                    slot = out_ring[c % SLOTS][:].rearrange("p r (q e) -> p r q e", e=E)
                    for i, j, n, place in chunks[c]:
                        if i % GROUP == 0 and j == i + 1:
                            dve.wait_ge(xw_copied, 2 * (t * GROUPS + i // GROUP + 1))
                        if i == 0:
                            for part in range(PARTS):
                                dve.wait_ge(x_landed[buf][part], 16 * (k + 1))
                                if first or part == PARTS - 1:
                                    n = CUTS[part + 1] - j
                                    last = multiply(slot, i, j, n, place)
                                    j, place = j + n, place + n
                                    if first and part == PARTS - 2:
                                        last.then_inc(early_ready, 1)
                        else:
                            last = multiply(slot, i, j, n, place)
                    last.then_inc(chunk_ready, 1)

            for buf in range(2):
                tile(0, buf, first=buf == 0)
            with dve.Fori(1, TILES // 2) as k:
                for buf in range(2):
                    tile(k, buf, first=False)


def kernel(r_x, L0_rec_W):
    import numpy as _np
    import concourse.bacc as _bacc
    from concourse import mybir as _mybir
    from concourse.bass_utils import run_bass_kernel_spmd as _run

    nc = _bacc.Bacc("TRN2", target_bir_lowering=False, num_devices=1)
    arrays, args = {}, []
    for name, a in (("x", r_x), ("W", L0_rec_W)):
        a = _np.ascontiguousarray(a)
        arrays[f"in_{name}_dram"] = a
        args.append(nc.dram_tensor(f"in_{name}_dram", a.shape, _mybir.dt.from_np(a.dtype), kind="ExternalInput").ap())
    batch, features, width = arrays["in_x_dram"].shape
    out = nc.dram_tensor("out_dram", (batch, features * (features - 1) // 2, width), _mybir.dt.float32,
                         kind="ExternalOutput").ap()
    pairwise_interaction_kernel(nc, *args, out)
    r = _run(nc, [arrays], core_ids=[0])
    return r.results[0]["out_dram"]
```
